# Optimizing a Trainium2 kernel written in Bass

```python
import numpy as np
import jax
import jax.numpy as jnp

def _softmax(x, axis=-1):
    return jax.nn.softmax(x, axis=axis)

def _gelu(x):
    return jax.nn.gelu(x, approximate=True)

def _silu(x):
    return jax.nn.silu(x)

def _sigmoid(x):
    return jax.nn.sigmoid(x)

def _layernorm(x, axis=-1, eps=1e-05):
    m = jnp.mean(x, axis=axis, keepdims=True)
    v = jnp.var(x, axis=axis, keepdims=True)
    return (x - m) / jnp.sqrt(v + eps)

def _scatter_add(tgt, idx, src, axis=0):
    return tgt.at[idx].add(src)

def _segment_sum(src, seg, n):
    return jax.ops.segment_sum(src, seg, n)
kernel_name = 'mk_early_fusion_d1_tok_img512_r4_d550f4'

def setup_inputs(seed: int=0):
    np.random.seed(seed)
    _w = jnp.asarray

    def _rec_inputs():
        import jax
        import jax.numpy as jnp
        _rk = jax.random.key(seed)
        x = -0.000356955 + 1 * jax.random.normal(jax.random.fold_in(_rk, 1), (32, 3, 64, 64), jnp.float32)
        txt = 0.0185972 + 1.43333 * jax.random.normal(jax.random.fold_in(_rk, 2), (32, 77, 128), jnp.float32)
        return (x, txt)
    x, txt = _rec_inputs()

    def _L0_tok_setup():
        import jax, jax.numpy as jnp
        import numpy as np
        key = jax.random.key(seed)
        k1, k2, k3 = jax.random.split(key, 3)
        B, C, H, W = (128, 3, 224, 224)
        E, p = (128, 16)
        K = C * p * p
        img = jax.random.normal(k1, (B, C, H, W), dtype=jnp.float32)
        w = jax.random.normal(k2, (E, K), dtype=jnp.float32) * (1.0 / np.sqrt(K))
        b = jax.random.normal(k3, (E,), dtype=jnp.float32)
        return {'img': img, 'w': w, 'b': b, 'patch_size': p}
    _L0_tok_all = _L0_tok_setup()
    _L0_tok_in = {k: v for k, v in _L0_tok_all.items() if k in ('w', 'b')}
    del _L0_tok_all

    def _L0_attn_setup():
        import jax, jax.numpy as jnp
        import numpy as np
        N_HEAD = 8
        D_HEAD = 64
        D_MODEL = 128
        SCALE = 1.0 / D_HEAD ** 0.5
        EPS = 1e-05

        def _layer_norm(x, gamma, beta):
            mu = jnp.mean(x, axis=-1, keepdims=True)
            var = jnp.var(x, axis=-1, keepdims=True)
            return (x - mu) * jax.lax.rsqrt(var + EPS) * gamma + beta
        key = jax.random.key(seed)
        ks = jax.random.split(key, 5)
        S, B = (512, 16)
        h = jax.random.normal(ks[0], (S, B, D_MODEL), dtype=jnp.float32)
        Wq = jax.random.normal(ks[1], (N_HEAD * D_HEAD, D_MODEL), dtype=jnp.float32) * 0.02
        Wkv = jax.random.normal(ks[2], (2 * N_HEAD * D_HEAD, D_MODEL), dtype=jnp.float32) * 0.02
        Wo = jax.random.normal(ks[3], (D_MODEL, N_HEAD * D_HEAD), dtype=jnp.float32) * 0.02
        ln_gamma = jnp.ones((D_MODEL,), dtype=jnp.float32)
        ln_beta = jnp.zeros((D_MODEL,), dtype=jnp.float32)
        return {'h': h, 'Wq': Wq, 'Wkv': Wkv, 'Wo': Wo, 'ln_gamma': ln_gamma, 'ln_beta': ln_beta}
    _L0_attn_all = _L0_attn_setup()
    _L0_attn_in = {k: v for k, v in _L0_attn_all.items() if k in ('Wq', 'Wkv', 'Wo', 'ln_gamma', 'ln_beta')}
    del _L0_attn_all

    def _L0_ffn_setup():
        import jax, jax.numpy as jnp
        import numpy as np
        B, S, D, O = (1, 512, 128, 128)
        H, QD, K, PK = (8, 64, 16, 64)
        N = PK * PK
        HALF = QD // 2

        def _l2norm(x):
            n = jnp.sqrt(jnp.sum(x * x, axis=-1, keepdims=True))
            return x / jnp.maximum(n, 1e-12)
        key = jax.random.key(seed)
        ks = jax.random.split(key, 9)
        return {'hidden_states': jax.random.normal(ks[0], (B, S, D), jnp.float32), 'Wq': jax.random.normal(ks[1], (H * QD, D), jnp.float32) * 0.02, 'bq': jnp.zeros((H * QD,), jnp.float32), 'ln_g': jnp.ones((QD,), jnp.float32), 'ln_b': jnp.zeros((QD,), jnp.float32), 'keys0': jax.random.normal(ks[2], (PK, HALF), jnp.float32) * 0.02, 'keys1': jax.random.normal(ks[3], (PK, HALF), jnp.float32) * 0.02, 'expert_down': jax.random.normal(ks[4], (N, D), jnp.float32) * 0.02, 'expert_up': jax.random.normal(ks[5], (N, O), jnp.float32) * 0.02}
    _L0_ffn_all = _L0_ffn_setup()
    _L0_ffn_in = {k: v for k, v in _L0_ffn_all.items() if k in ('Wq', 'bq', 'ln_g', 'ln_b', 'keys0', 'keys1', 'expert_down', 'expert_up')}
    del _L0_ffn_all
    return {'x': x, 'txt': txt, 'L0_tok_w': _L0_tok_in['w'], 'L0_tok_b': _L0_tok_in['b'], 'L0_attn_Wq': _L0_attn_in['Wq'], 'L0_attn_Wkv': _L0_attn_in['Wkv'], 'L0_attn_Wo': _L0_attn_in['Wo'], 'L0_attn_ln_gamma': _L0_attn_in['ln_gamma'], 'L0_attn_ln_beta': _L0_attn_in['ln_beta'], 'L0_ffn_Wq': _L0_ffn_in['Wq'], 'L0_ffn_bq': _L0_ffn_in['bq'], 'L0_ffn_ln_g': _L0_ffn_in['ln_g'], 'L0_ffn_ln_b': _L0_ffn_in['ln_b'], 'L0_ffn_keys0': _L0_ffn_in['keys0'], 'L0_ffn_keys1': _L0_ffn_in['keys1'], 'L0_ffn_expert_down': _L0_ffn_in['expert_down'], 'L0_ffn_expert_up': _L0_ffn_in['expert_up']}

def reference(x, txt, L0_tok_w, L0_tok_b, L0_attn_Wq, L0_attn_Wkv, L0_attn_Wo, L0_attn_ln_gamma, L0_attn_ln_beta, L0_ffn_Wq, L0_ffn_bq, L0_ffn_ln_g, L0_ffn_ln_b, L0_ffn_keys0, L0_ffn_keys1, L0_ffn_expert_down, L0_ffn_expert_up):
    import jax
    import jax.numpy as jnp

    def _L0_tok_ref(img, w, b, patch_size):
        import jax, jax.numpy as jnp
        import numpy as np
        B, C, H, W = img.shape
        p = patch_size
        Hp, Wp = (H // p, W // p)
        S = Hp * Wp
        patches = img.reshape(B, C, Hp, p, Wp, p)
        patches = patches.transpose(0, 2, 4, 1, 3, 5).reshape(B, S, C * p * p)
        out = jnp.einsum('bsk,ek->bse', patches, w) + b
        return out

    def _L0_attn_ref(h, Wq, Wkv, Wo, ln_gamma, ln_beta):
        import jax, jax.numpy as jnp
        import numpy as np
        N_HEAD = 8
        D_HEAD = 64
        D_MODEL = 128
        SCALE = 1.0 / D_HEAD ** 0.5
        EPS = 1e-05

        def _layer_norm(x, gamma, beta):
            mu = jnp.mean(x, axis=-1, keepdims=True)
            var = jnp.var(x, axis=-1, keepdims=True)
            return (x - mu) * jax.lax.rsqrt(var + EPS) * gamma + beta
        S, B, D = h.shape
        BH = B * N_HEAD
        q = h @ Wq.T
        kv = h @ Wkv.T
        k, v = jnp.split(kv, 2, axis=-1)
        q = jax.nn.elu(q) + 1.0
        k = jax.nn.elu(k) + 1.0
        q = q.reshape(S, BH, D_HEAD)
        k = k.reshape(S, BH, D_HEAD)
        v = v.reshape(S, BH, D_HEAD)

        def step(state, xs):
            kt, vt, qt = xs
            state = state + vt[:, :, None] * kt[:, None, :]
            out = jnp.einsum('bij,bj->bi', state, qt)
            return (state, out)
        init = jnp.zeros((BH, D_HEAD, D_HEAD), dtype=h.dtype)
        _, outs = jax.lax.scan(step, init, (k, v, q))
        layer_out = (SCALE * outs).reshape(S, B, N_HEAD * D_HEAD)
        attn_out = layer_out @ Wo.T
        return _layer_norm(h + attn_out, ln_gamma, ln_beta)

    def _L0_ffn_ref(hidden_states, Wq, bq, ln_g, ln_b, keys0, keys1, expert_down, expert_up):
        import jax, jax.numpy as jnp
        import numpy as np
        B, S, D, O = (1, 512, 128, 128)
        H, QD, K, PK = (8, 64, 16, 64)
        N = PK * PK
        HALF = QD // 2

        def _l2norm(x):
            n = jnp.sqrt(jnp.sum(x * x, axis=-1, keepdims=True))
            return x / jnp.maximum(n, 1e-12)
        b, s, d = hidden_states.shape
        q = (hidden_states @ Wq.T + bq).reshape(b, s, H, QD)
        mu = jnp.mean(q, axis=-1, keepdims=True)
        var = jnp.mean((q - mu) ** 2, axis=-1, keepdims=True)
        q = (q - mu) / jnp.sqrt(var + 1e-05) * ln_g + ln_b
        q0, q1 = (q[..., :HALF], q[..., HALF:])
        s0 = jnp.einsum('bshq,eq->bshe', _l2norm(q0), _l2norm(keys0))
        s1 = jnp.einsum('bshq,eq->bshe', _l2norm(q1), _l2norm(keys1))
        sc0, ix0 = jax.lax.top_k(s0, K)
        sc1, ix1 = jax.lax.top_k(s1, K)
        cs = (sc0[..., :, None] + sc1[..., None, :]).reshape(b, s, H, K * K)
        ci = (ix0[..., :, None] + ix1[..., None, :]).reshape(b, s, H, K * K)
        fs, pos = jax.lax.top_k(cs, K)
        fi = jnp.take_along_axis(ci, pos, axis=-1)
        w = jax.nn.softmax(fs, axis=-1)
        down = expert_down[fi]
        up = expert_up[fi]
        inner = jnp.einsum('bsd,bshkd->bshk', hidden_states, down)
        act = jax.nn.gelu(inner, approximate=False)
        out = jnp.einsum('bshk,bshko->bso', act * w, up)
        return out
    h = _L0_tok_ref(x, L0_tok_w, L0_tok_b, 16)
    h = jnp.concatenate([h, txt], axis=1)
    h = h + _L0_attn_ref(_layernorm(h, axis=-1), L0_attn_Wq, L0_attn_Wkv, L0_attn_Wo, L0_attn_ln_gamma, L0_attn_ln_beta)
    h = h + _L0_ffn_ref(_layernorm(h, axis=-1), L0_ffn_Wq, L0_ffn_bq, L0_ffn_ln_g, L0_ffn_ln_b, L0_ffn_keys0, L0_ffn_keys1, L0_ffn_expert_down, L0_ffn_expert_up)
    return h

_drawn_inputs = setup_inputs


def setup_inputs(seed=0):
    import zlib

    import numpy as np

    out = dict(_drawn_inputs(seed))
    spreads = {'L0_attn_ln_gamma': (1.0, 0.2),
     'L0_attn_ln_beta': (0.0, 0.1),
     'L0_ffn_bq': (0.0, 0.8),
     'L0_ffn_ln_g': (1.0, 0.6),
     'L0_ffn_ln_b': (0.0, 0.8)}
    factors = {'L0_attn_Wq': 4.593,
     'L0_ffn_Wq': 8.0,
     'L0_ffn_keys0': 8.0,
     'L0_ffn_keys1': 8.0,
     'L0_ffn_expert_down': 8.0,
     'L0_ffn_expert_up': 8.0}
    for name, (base, spread) in spreads.items():
        noise = np.random.default_rng([zlib.crc32(name.encode()), seed]).standard_normal(out[name].shape)
        drawn = base * np.exp(spread * noise) if base else spread * noise
        out[name] = jnp.asarray(drawn.astype(out[name].dtype))
    for name, factor in factors.items():
        out[name] = (out[name] * factor).astype(out[name].dtype)
    return out
```

```python
from contextlib import ExitStack

import concourse.bass as bass
from concourse import mybir

F32 = mybir.dt.float32
BF16 = mybir.dt.bfloat16
U32 = mybir.dt.uint32
ALU = mybir.AluOpType
ACT = mybir.ActivationFunctionType
AX_X = mybir.AxisListType.X

P = 128
STEPS = 32
NPATCH = 16
NTXT = 77
NPOS = NPATCH + NTXT
BPT = P // STEPS
TILES = -(-NPOS // BPT)
TOK_TILES = NPATCH // BPT
KCH = 6
D = 128
NH = 8
DH = 64
CH = NH * DH // P
PK = 64
TOPK = 16
LISTS = 2 * NH
NSLOT = 32
HI, LO = 4, 32
SPLIT = 3
GRP = 4
NGRP = P // GRP
SCALE = 0.125
EPS = 1e-5
TINY = 1e-24
LOW = -1e30
MAGIC = 1.5 * 2.0 ** 23

CELLS = [(0, 1, 16, 0), (1, 1, 8, 16), (2, 2, 5, 24), (4, 4, 3, 34), (8, 8, 1, 46)]
NCELL = 54
FOLDS = [(16, 5, 1, 15), (24, 5, 2, 14), (34, 3, 4, 12), (46, 1, 8, 8), (35, 3, 4, 16 + 5)]
KEPT = [(0, 1, 1, 16, 0), (17, 1, 1, 7, 16), (25, 2, 5, 4, 23), (36, 1, 1, 1, 31)]

SEMS = """weights h_loaded h_out_stored setup_pe setup_act setup_dve setup_pool tok_done tok_copied h_taken
ln1_stats ln1_aggr ln1_std ln1_rstd hn hnT_ps hnT qk_ps v_ps qk_neg qk_exp qk_pos qk v at_ps at_copied at_masked ot_ps ot
attn_ps y ln2_stats ln2_aggr ln2_std ln2_rstd y_norm y_gamma y_beta h2 ln3_stats ln3_aggr ln3_std ln3_rstd hn2
hn2T_ps hn2T qc_ps sq var_ps sigma vT_ps vT vsq scores_ps norms_ps norms_copied norm_a norm_b norm_std norm_r
scores_sb inner_ps expert_act handed top_a idx_a rest_a top_b idx_b idx_f sorted_s shifted exps cells_a cells_w
fin_a fin_rest fin_b fin_last sel masked folded kept zsum zrec wnorm hi_a hi_f lo_f w1 r1 w2 r2 w3 ktA_ps ktA ktB_ps ktB
oh_lo oh_hi wh hist_ps hist_sb g_a g_sum gated out_ps out_sb dve_passed pool_passed""".split()


def build(nc, xT, txt, identity, causal, centre, ind8, ind4, headmask, tok_wT, tok_b, wqkT, wvT, woT, gamma, beta,
          ffn_wq, ffn_bq, ln_g, ln_b, keys, downT, up, groupmask, out):
    with ExitStack() as ctx:
        def sb(name, shape, dt=F32):
            return ctx.enter_context(nc.sbuf_tensor(name, shape, dt))

        S = {name: ctx.enter_context(nc.semaphore("s_" + name)) for name in SEMS}

        wide = ctx.enter_context(nc.psum_tensor("wide", [P, 2, 512], F32))
        mid = ctx.enter_context(nc.psum_tensor("mid", [P, 512], F32))
        small = ctx.enter_context(nc.psum_tensor("small", [P, 4, 128], F32))
        fourth = ctx.enter_context(nc.psum_tensor("fourth", [P, 512], F32))
        fifth = ctx.enter_context(nc.psum_tensor("fifth", [P, 512], F32))
        hist = ctx.enter_context(nc.psum_tensor("hist", [P, 2, 512], F32))

        ident = sb("ident", [P, P])
        ident_bf = sb("ident_bf", [P, P], BF16)
        mask = sb("mask", [P, P])
        cen = sb("cen", [P, P])
        ceng = sb("ceng", [P, P])
        i8 = sb("i8", [P, CH, NH])
        i4 = sb("i4", [P, 4])
        hmask = sb("hmask", [NH, NH * DH])
        xts = sb("xts", [P, KCH, TOK_TILES * P])
        wtok = sb("wtok", [P, KCH, D])
        btok = sb("btok", [1, D])
        ones = sb("ones", [1, P])
        htok = sb("htok", [P, TOK_TILES, D])
        wqk = sb("wqk", [P, 2 * NH * DH])
        wv = sb("wv", [P, NH * DH])
        wo = sb("wo", [P, CH, D])
        gam = sb("gam", [P, D])
        bet = sb("bet", [P, D])
        fwq = sb("fwq", [P, CH, D])
        fbq = sb("fbq", [P, CH])
        grow = sb("grow", [P, P])
        brow = sb("brow", [NH, NH * DH])
        wcT = sb("wcT", [P, CH, P])
        wgT = sb("wgT", [P, CH, P])
        bc = sb("bc", [1, CH * P])
        bcg = sb("bcg", [1, CH * P])
        bh = sb("bh", [NH, CH * P])
        kraw = sb("kraw", [PK, 2, 2, 32])
        ksq = sb("ksq", [PK, 4, 32])
        knorm = sb("knorm", [PK, 4])
        khat = sb("khat", [PK, P])
        kbd = sb("kbd", [P, 4, PK])
        down = sb("down", [P, HI, P])
        qmask = sb("qmask", [P, GRP])
        ups = sb("ups", [P, HI, D])
        eps = sb("eps", [P, 1])

        h_in = sb("h_in", [P, D])
        h_cur = sb("h_cur", [P, D])
        stats = sb("stats", [P, 3, 6])
        mv = sb("mv", [P, 3, 2])
        std = sb("std", [P, 3])
        rstd = sb("rstd", [P, 3])
        hn = sb("hn", [P, D])
        hnT = sb("hnT", [P, P])
        neg = sb("neg", [P, 1024])
        ex = sb("ex", [P, 1024])
        pos = sb("pos", [P, 1024])
        qk = sb("qk", [P, 2 * CH, P])
        v = sb("v", [P, NH * DH])
        at = sb("at", [P, NH, P])
        atm = sb("atm", [P, NH, P])
        ot = sb("ot", [P, CH, P])
        y = sb("y", [P, D])
        yn = sb("yn", [P, D])
        yg = sb("yg", [P, D])
        yb = sb("yb", [P, D])
        h2 = sb("h2", [P, D])
        hn2 = sb("hn2", [P, D])
        hn2T = sb("hn2T", [P, P])
        sq = sb("sq", [P, CH, P])
        sigma = sb("sigma", [NH, P])
        vT = sb("vT", [P, CH, P])
        vsq = sb("vsq", [P, CH, P])
        var_n = sb("var_n", [P, 24])
        floor_n = sb("floor_n", [P, NH])
        norm2 = sb("norm2", [P, NH, 2])
        normv = sb("normv", [P, LISTS])
        normr = sb("normr", [P, LISTS])
        scores = sb("scores", [P, LISTS, PK])
        eact = sb("eact", [P, HI, P])

        h2b = sb("h2b", [P, D])
        eactb = sb("eactb", [P, HI, P])
        normb = sb("normb", [P, LISTS])
        rest = sb("rest", [P, LISTS, PK])
        top = sb("top", [P, LISTS, TOPK])
        idx = sb("idx", [P, LISTS, TOPK], U32)
        sv = sb("sv", [P, 2, LISTS, TOPK])
        sh = sb("sh", [P, LISTS, TOPK])
        es = sb("es", [P, LISTS, TOPK])
        cell = sb("cell", [P, 3, NH, NCELL])
        crest = sb("crest", [P, NH, NCELL])
        clast = sb("clast", [P, NH, NCELL])
        ctop = sb("ctop", [P, NH, TOPK])
        sel = sb("sel", [P, NH, NCELL])
        chosen = sb("chosen", [P, 2 * NH, NCELL])
        slot = sb("slot", [P, 2, NH, NSLOT])
        zs = sb("zs", [P, NH])
        zr = sb("zr", [P, NH])
        wn = sb("wn", [P, NH * NSLOT])
        r1 = sb("r1", [P, NH * NSLOT])
        r2 = sb("r2", [P, NH * NSLOT])
        hi0 = sb("hi0", [P, NH * NSLOT])
        parts = sb("parts", [P, SPLIT + 2, NH * NSLOT], BF16)
        kt = sb("kt", [P, SPLIT + 2, 2, P], BF16)
        ohlo = sb("ohlo", [P, 2 * NGRP, LO, GRP], BF16)
        ohhi = sb("ohhi", [P, HI, 2 * P], BF16)
        wh = sb("wh", [P, SPLIT, HI, 2 * P], BF16)
        hs = sb("hs", [P, SPLIT, HI, P])
        gs = sb("gs", [P, 2, HI * P])
        gated = sb("gated", [P, HI, P])
        out_sb = sb("out_sb", [P, D])

        block = ctx.enter_context(nc.Block())
        WLOADS = [(ident, identity), (mask, causal), (cen, centre), (i8, ind8), (i4, ind4), (hmask, headmask),
                  (xts, xT), (wtok, tok_wT), (btok, tok_b), (wqk, wqkT), (wv, wvT), (wo, woT),
                  (gam, gamma.broadcast_to([P, D])), (bet, beta.broadcast_to([P, D])), (fwq, ffn_wq), (fbq, ffn_bq),
                  (grow, ln_g.broadcast_to([P, P])), (brow, ln_b.broadcast_to([NH, NH * DH])),
                  (kraw, keys), (down, downT), (ups, up), (qmask, groupmask)]

        def reuse(eng, sem, count):
            if not (isinstance(count, int) and count == 0):
                eng.wait_ge(sem, count)

        def stand_alone(eng):
            eng.sem_inc(S["dve_passed"] if eng is nc.vector else S["pool_passed"], 1)

        @block.sync
        def _(sp):
            for dst, src in WLOADS:
                sp.dma_start(dst[:], src).then_inc(S["weights"], 16)

            def load_patch(t):
                for b in range(BPT):
                    rows = slice(b * STEPS, (b + 1) * STEPS)
                    sp.dma_start(h_in[rows, :], htok[rows, t, :]).then_inc(S["h_loaded"], 16)

            def load_txt(first):
                for b in range(BPT):
                    sp.dma_start(h_in[b * STEPS:(b + 1) * STEPS, :],
                                 txt[:, bass.ds(first + b, 1), :].rearrange("s b d -> (s b) d")).then_inc(S["h_loaded"], 16)

            def store(first):
                for b in range(BPT):
                    sp.dma_start(out[:, bass.ds(first + b, 1), :].rearrange("s b d -> (s b) d"),
                                 out_sb[b * STEPS:(b + 1) * STEPS, :]).then_inc(S["h_out_stored"], 16)

            sp.wait_ge(S["tok_copied"], TOK_TILES)
            load_patch(0)
            sp.wait_ge(S["h_taken"], 1)
            load_patch(1)
            for i in range(TOK_TILES - 2):
                sp.wait_ge(S["h_taken"], i + 2)
                load_patch(i + 2)
                sp.wait_ge(S["out_sb"], i + 1)
                store(BPT * i)
            with sp.Fori(TOK_TILES - 2, TILES - 3) as i:
                sp.wait_ge(S["h_taken"], i + 2)
                load_txt(i * BPT + (2 * BPT - NPATCH))
                sp.wait_ge(S["out_sb"], i + 1)
                store(i * BPT)
            sp.wait_ge(S["h_taken"], TILES - 1)
            load_txt(NTXT - BPT)
            sp.wait_ge(S["out_sb"], TILES - 2)
            store(BPT * (TILES - 3))
            sp.wait_ge(S["out_sb"], TILES - 1)
            store(BPT * (TILES - 2))
            sp.wait_ge(S["out_sb"], TILES)
            sp.dma_start(out[:, NPOS - 1:NPOS, :].rearrange("s b d -> (s b) d"),
                         out_sb[P - STEPS:P, :]).then_inc(S["h_out_stored"], 16)
            sp.wait_ge(S["h_out_stored"], 16 * (BPT * (TILES - 1) + 1))

        @block.tensor
        def _(pe):
            mm = nc.tensor.matmul
            pe.wait_ge(S["weights"], 16 * len(WLOADS))
            pe.wait_ge(S["setup_pool"], 4)
            for t in range(TOK_TILES):
                if t:
                    reuse(pe, S["tok_copied"], t)
                for k in range(KCH):
                    mm(mid[:, 0:D], xts[:, k, t * P:(t + 1) * P], wtok[:, k, :], start=(k == 0), stop=False)
                mm(mid[:, 0:D], ones[:], btok[:], start=False, stop=True).then_inc(S["tok_done"], 1)
            for c in range(CH):
                last = mm(wide[:, 0, c * P:(c + 1) * P], fwq[:, c, :], cen[:], start=True, stop=True)
            last.then_inc(S["setup_pe"], 1)
            pe.wait_ge(S["setup_dve"], 1)
            for c in range(CH):
                mm(wide[:, 1, c * P:(c + 1) * P], fwq[:, c, :], ceng[:], start=True, stop=True)
            for c in range(CH):
                mm(fourth[0:1, c * P:(c + 1) * P], fbq[:, c:c + 1], cen[:], start=True, stop=True)
            for c in range(CH):
                last = mm(fifth[0:1, c * P:(c + 1) * P], fbq[:, c:c + 1], ceng[:], start=True, stop=True)
            last.then_inc(S["setup_pe"], 1)
            pe.wait_ge(S["setup_dve"], 6)
            nc.tensor.transpose(small[:, 0, 0:PK], khat[:], ident[0:PK, 0:PK]).then_inc(S["setup_pe"], 1)
            pe.wait_ge(S["setup_dve"], 7)
            pe.wait_ge(S["setup_act"], 10)

            def front(t):
                pe.wait_ge(S["hn"], t + 1)
                reuse(pe, S["expert_act"], t)
                nc.tensor.transpose(small[:, 0, :], hn[:], ident[:]).then_inc(S["hnT_ps"], 1)
                pe.wait_ge(S["hnT"], t + 1)
                reuse(pe, S["scores_sb"], t)
                for c in range(2 * CH):
                    last = mm(wide[:, c // CH, (c % CH) * P:(c % CH + 1) * P], wqk[:, c * P:(c + 1) * P], hnT[:],
                              start=True, stop=True)
                last.then_inc(S["qk_ps"], 1)
                reuse(pe, S["sq"], t)
                mm(mid[:], hnT[:], wv[:], start=True, stop=True).then_inc(S["v_ps"], 1)
                pe.wait_ge(S["qk"], t + 1)
                for h in range(NH):
                    r = DH * (h % 2)
                    last = mm(wide[:, h % 2, (h // 2) * P:(h // 2 + 1) * P], qk[r:r + DH, CH + h // 2, :],
                              qk[r:r + DH, h // 2, :], start=True, stop=True)
                last.then_inc(S["at_ps"], 1)
                pe.wait_ge(S["at_masked"], t + 1)
                pe.wait_ge(S["v"], t + 1)
                for h in range(NH):
                    r = DH * (h % 2)
                    last = mm(mid[r:r + DH, (h // 2) * P:(h // 2 + 1) * P], v[:, h * DH:(h + 1) * DH],
                              atm[:, (h % 2) * CH + h // 2, :], start=True, stop=True)
                last.then_inc(S["ot_ps"], 1)
                pe.wait_ge(S["ot"], t + 1)
                for c in range(CH):
                    last = mm(small[:, 1, :], ot[:, c, :], wo[:, c, :], start=(c == 0), stop=(c == CH - 1))
                last.then_inc(S["attn_ps"], 1)
                pe.wait_ge(S["hn2"], t + 1)
                nc.tensor.transpose(small[:, 2, :], hn2[:], ident[:]).then_inc(S["hn2T_ps"], 1)
                pe.wait_ge(S["hn2T"], t + 1)
                for c in range(CH):
                    mm(mid[:, c * P:(c + 1) * P], wcT[:, c, :], hn2T[:], start=True, stop=False)
                    last = mm(mid[:, c * P:(c + 1) * P], bc[:, c * P:(c + 1) * P], ones[:], start=False, stop=True)
                last.then_inc(S["qc_ps"], 1)
                pe.wait_ge(S["sq"], t + 1)
                reuse(pe, S["norms_copied"], t)
                for c in range(CH):
                    last = mm(small[0:NH, 3, :], i8[:, c, :], sq[:, c, :], start=(c == 0), stop=(c == CH - 1))
                last.then_inc(S["var_ps"], 1)
                pe.wait_ge(S["sigma"], t + 1)
                for c in range(CH):
                    o = fourth[:, c * P:(c + 1) * P]
                    mm(o, wgT[:, c, :], hn2T[:], start=True, stop=False)
                    mm(o, bcg[:, c * P:(c + 1) * P], ones[:], start=False, stop=False)
                    last = mm(o, bh[:, c * P:(c + 1) * P], sigma[:], start=False, stop=True)
                last.then_inc(S["vT_ps"], 1)
                pe.wait_ge(S["vT"], t + 1)
                for c in range(CH):
                    last = mm(wide[:, c // 2, (c % 2) * 256:(c % 2 + 1) * 256], vT[:, c, :],
                              kbd[:].rearrange("p a b -> p (a b)"), start=True, stop=True)
                last.then_inc(S["scores_ps"], 1)
                pe.wait_ge(S["vsq"], t + 1)
                for c in range(CH):
                    mm(small[:, 3, 2 * c:2 * c + 2], sq[:, c, :], i8[:, 0, 0:2], start=True, stop=True)
                    last = mm(small[:, 3, 8 + 4 * c:12 + 4 * c], vsq[:, c, :], i4[:], start=True, stop=True)
                last.then_inc(S["norms_ps"], 1)
                for i in range(HI):
                    last = mm(fourth[:, i * P:(i + 1) * P], down[:, i, :], hn2T[:], start=True, stop=True)
                last.then_inc(S["inner_ps"], 1)

            def back(t):
                pe.wait_ge(S["w3"], t + 1)
                pe.wait_ge(S["lo_f"], t + 1)
                reuse(pe, S["hist_sb"], 4 * t)
                reuse(pe, S["out_sb"], t)
                kta = fifth[:].bitcast(BF16)
                ktb = hist[:, 0, :].bitcast(BF16)
                for s in range(SPLIT):
                    for c in range(2):
                        last = nc.tensor.transpose(kta[:, (2 * s + c) * P:(2 * s + c + 1) * P],
                                                   parts[:, s, c * P:(c + 1) * P], ident_bf[:])
                last.then_inc(S["ktA_ps"], 1)
                for s in range(2):
                    for c in range(2):
                        last = nc.tensor.transpose(ktb[:, (2 * s + c) * P:(2 * s + c + 1) * P],
                                                   parts[:, SPLIT + s, c * P:(c + 1) * P], ident_bf[:])
                last.then_inc(S["ktB_ps"], 1)
                pe.wait_ge(S["oh_lo"], t + 1)
                pe.wait_ge(S["wh"], t + 1)
                for half in range(2):
                    if half:
                        pe.wait_ge(S["hist_sb"], 4 * t + 2)
                    for g in range(NGRP // 2):
                        tok = (half * NGRP // 2 + g) * GRP
                        for c in range(2):
                            last = mm(hist[:, g // 8, (g % 8) * 48:(g % 8) * 48 + 48],
                                      ohlo[:, c * NGRP + half * NGRP // 2 + g].rearrange("p l q -> p (l q)"),
                                      wh[:].rearrange("p s i t -> p (s i) t")[:, :, c * P + tok:c * P + tok + GRP],
                                      start=(c == 0), stop=(c == 1))
                    last.then_inc(S["hist_ps"], 1)
                pe.wait_ge(S["gated"], t + 1)
                for i in range(HI):
                    last = mm(fifth[:, 0:D], gated[:, i, :], ups[:, i, :], start=(i == 0), stop=(i == HI - 1))
                last.then_inc(S["out_ps"], 1)

            front(0)
            front(1)
            back(0)
            with pe.Fori(1, TILES - 1) as i:
                front(i + 1)
                back(i)
            back(TILES - 1)

        @block.scalar
        def _(act):
            A = nc.scalar.activation
            act.wait_ge(S["setup_pool"], 4)
            for t in range(TOK_TILES):
                act.wait_ge(S["tok_done"], t + 1)
                A(htok[:, t, :], mid[:, 0:D], ACT.Copy).then_inc(S["tok_copied"], 1)
            act.wait_ge(S["weights"], 16 * len(WLOADS))
            A(ident_bf[:], ident[:], ACT.Copy).then_inc(S["setup_act"], 1)
            act.wait_ge(S["setup_pe"], 1)
            A(wcT[:].rearrange("p c m -> p (c m)"), wide[:, 0, :], ACT.Copy).then_inc(S["setup_act"], 1)
            act.wait_ge(S["setup_pe"], 2)
            A(wgT[:].rearrange("p c m -> p (c m)"), wide[:, 1, :], ACT.Copy).then_inc(S["setup_act"], 1)
            A(bc[:], fourth[0:1, :], ACT.Copy).then_inc(S["setup_act"], 1)
            A(bcg[:], fifth[0:1, :], ACT.Copy).then_inc(S["setup_act"], 1)
            act.wait_ge(S["setup_dve"], 3)
            A(knorm[:], knorm[:], ACT.Sqrt).then_inc(S["setup_act"], 1)
            act.wait_ge(S["setup_pe"], 3)
            for q in range(4):
                A(kbd[32 * q:32 * q + 32, q, :], small[32 * q:32 * q + 32, 0, 0:PK], ACT.Copy).then_inc(S["setup_act"], 1)

            def front(t):
                act.wait_ge(S["ln1_aggr"], t + 1)
                A(std[:, 0:1], mv[:, 0, 1:2], ACT.Sqrt, bias=eps[:]).then_inc(S["ln1_std"], 1)
                act.wait_ge(S["hnT_ps"], t + 1)
                A(hnT[:], small[:, 0, :], ACT.Copy).then_inc(S["hnT"], 1)
                act.wait_ge(S["qk_ps"], t + 1)
                reuse(act, S["qk"], t)
                wf = wide[:].rearrange("p a b -> p (a b)")
                A(neg[:], wf, ACT.Relu, scale=-1.0).then_inc(S["qk_neg"], 1)
                A(pos[:], wf, ACT.Relu).then_inc(S["qk_pos"], 1)
                act.wait_ge(S["qk_neg"], t + 1)
                A(ex[:], neg[:], ACT.Exp, scale=-1.0).then_inc(S["qk_exp"], 1)
                act.wait_ge(S["v_ps"], t + 1)
                A(v[:], mid[:], ACT.Copy).then_inc(S["v"], 1)
                act.wait_ge(S["at_ps"], t + 1)
                A(at[:].rearrange("p h i -> p (h i)"), wf, ACT.Copy).then_inc(S["at_copied"], 1)
                act.wait_ge(S["ot_ps"], t + 1)
                A(ot[:].rearrange("p c i -> p (c i)"), mid[:], ACT.Copy, scale=SCALE).then_inc(S["ot"], 1)
                act.wait_ge(S["ln2_aggr"], t + 1)
                A(std[:, 1:2], mv[:, 1, 1:2], ACT.Sqrt, bias=eps[:]).then_inc(S["ln2_std"], 1)
                act.wait_ge(S["ln3_aggr"], t + 1)
                A(std[:, 2:3], mv[:, 2, 1:2], ACT.Sqrt, bias=eps[:]).then_inc(S["ln3_std"], 1)
                act.wait_ge(S["hn2T_ps"], t + 1)
                A(hn2T[:], small[:, 2, :], ACT.Copy).then_inc(S["hn2T"], 1)
                act.wait_ge(S["qc_ps"], t + 1)
                A(sq[:].rearrange("p c i -> p (c i)"), mid[:], ACT.Square).then_inc(S["sq"], 1)
                act.wait_ge(S["var_ps"], t + 1)
                A(sigma[:], small[0:NH, 3, :], ACT.Sqrt, bias=eps[0:NH, :]).then_inc(S["sigma"], 1)
                act.wait_ge(S["vT_ps"], t + 1)
                A(vT[:].rearrange("p c i -> p (c i)"), fourth[:], ACT.Copy).then_inc(S["vT"], 1)
                A(vsq[:].rearrange("p c i -> p (c i)"), fourth[:], ACT.Square).then_inc(S["vsq"], 1)
                act.wait_ge(S["norms_ps"], t + 1)
                A(var_n[:], small[:, 3, 0:24], ACT.Copy).then_inc(S["norms_copied"], 1)
                act.wait_ge(S["inner_ps"], t + 1)
                reuse(act, S["handed"], 3 * t)
                A(eact[:].rearrange("p i g -> p (i g)"), fourth[:], ACT.Gelu).then_inc(S["expert_act"], 1)
                act.wait_ge(S["scores_ps"], t + 1)
                reuse(act, S["rest_a"], LISTS * t)
                A(scores[:].rearrange("p l e -> p (l e)"), wf, ACT.Copy).then_inc(S["scores_sb"], 1)

            def front_late(t):
                act.wait_ge(S["norm_b"], t + 1)
                reuse(act, S["norm_r"], t)
                A(normv[:], norm2[:].rearrange("p h l -> p (h l)"), ACT.Sqrt).then_inc(S["norm_std"], 1)

            def back(t):
                act.wait_ge(S["idx_a"], LISTS * t + LISTS)
                act.wait_ge(S["idx_b"], LISTS * t + LISTS)
                reuse(act, S["cells_a"], len(CELLS) * t)
                A(sv[:, 1].rearrange("p l k -> p (l k)"), idx[:].rearrange("p l k -> p (l k)"),
                  ACT.Copy).then_inc(S["idx_f"], 1)
                act.wait_ge(S["shifted"], t + 1)
                reuse(act, S["cells_w"], len(CELLS) * t)
                A(es[:].rearrange("p l k -> p (l k)"), sh[:].rearrange("p l k -> p (l k)"),
                  ACT.Exp).then_inc(S["exps"], 1)
                act.wait_ge(S["folded"], len(FOLDS) * t + len(FOLDS))
                reuse(act, S["lo_f"], t)
                reuse(act, S["wnorm"], t)
                s16 = slot[:].rearrange("p k h s -> p (k h) s")
                for at0, rows, step, cols, dst in KEPT:
                    if rows == 1:
                        A(s16[:, :, dst:dst + cols], chosen[:, :, at0:at0 + cols], ACT.Copy).then_inc(S["kept"], 1)
                    else:
                        A(s16[:, :, dst:dst + rows * cols].rearrange("p k (r c) -> p k r c", r=rows),
                          chosen[:, :, at0:at0 + rows * step].rearrange("p k (r c) -> p k r c", r=rows)[:, :, :, 0:cols],
                          ACT.Copy).then_inc(S["kept"], 1)
                act.wait_ge(S["wnorm"], t + 1)
                reuse(act, S["ktB_ps"], t)
                A(parts[:, 0, :], wn[:], ACT.Copy).then_inc(S["w1"], 1)
                act.wait_ge(S["r1"], t + 1)
                A(parts[:, 1, :], r1[:], ACT.Copy).then_inc(S["w2"], 1)
                act.wait_ge(S["ktB_ps"], t + 1)
                reuse(act, S["oh_lo"], t)
                reuse(act, S["wh"], t)
                A(kt[:, SPLIT:SPLIT + 2].rearrange("p s c t -> p (s c t)"), hist[:, 0, :].bitcast(BF16)[:, 0:4 * P],
                  ACT.Copy).then_inc(S["ktB"], 1)
                A(kt[:, 0:SPLIT].rearrange("p s c t -> p (s c t)"), fifth[:].bitcast(BF16)[:, 0:6 * P],
                  ACT.Copy).then_inc(S["ktA"], 1)
                reuse(act, S["g_sum"], t)
                for half in range(2):
                    act.wait_ge(S["hist_ps"], 2 * t + half + 1)
                    for b in range(2):
                        tok = (2 * half + b) * 8 * GRP
                        A(hs[:, :, :, tok:tok + 8 * GRP].rearrange("p s i (g q) -> p g (s i) q", q=GRP),
                          hist[:, b, 0:384].rearrange("p (g m q) -> p g m q", g=8, q=GRP), ACT.Copy).then_inc(S["hist_sb"], 1)

            front(0)
            front_late(0)
            front(1)
            back(0)
            front_late(1)
            with act.Fori(1, TILES - 1) as i:
                front(i + 1)
                back(i)
                front_late(i + 1)
            back(TILES - 1)

        @block.vector
        def _(dve):
            V = nc.vector
            dve.wait_ge(S["weights"], 16 * len(WLOADS))
            V.tensor_tensor(ceng[:], cen[:], grow[:], ALU.mult).then_inc(S["setup_dve"], 1)
            V.tensor_tensor(ksq[:], kraw[:].rearrange("p a b c -> p (a b) c"), kraw[:].rearrange("p a b c -> p (a b) c"),
                            ALU.mult).then_inc(S["setup_dve"], 1)
            dve.wait_ge(S["setup_dve"], 2)
            V.tensor_reduce(knorm[:], ksq[:], AX_X, ALU.add).then_inc(S["setup_dve"], 1)
            dve.wait_ge(S["setup_act"], 6)
            V.tensor_scalar(knorm[:], knorm[:], 1e-12, None, ALU.max).then_inc(S["setup_dve"], 1)
            dve.wait_ge(S["setup_dve"], 4)
            V.reciprocal(knorm[:], knorm[:]).then_inc(S["setup_dve"], 1)
            dve.wait_ge(S["setup_dve"], 5)
            V.tensor_tensor(khat[:].rearrange("p (a b) -> p a b", a=4), kraw[:].rearrange("p a b c -> p (a b) c"),
                            knorm[:].rearrange("p (a o) -> p a o", o=1).broadcast_to([PK, 4, 32]),
                            ALU.mult).then_inc(S["setup_dve"], 1)
            V.tensor_tensor(bh[:], brow[:], hmask[:], ALU.mult).then_inc(S["setup_dve"], 1)
            dve.wait_ge(S["setup_pool"], 4)

            def norm_stats(k, x, name, t):
                V.bn_stats(stats[:, k, :], x).then_inc(S[name + "_stats"], 1)
                dve.wait_ge(S[name + "_stats"], t + 1)
                stand_alone(dve)
                V.bn_aggr(mv[:, k, :], stats[:, k, :]).then_inc(S[name + "_aggr"], 1)

            def normalise(k, dst, x, name, done, t):
                dve.wait_ge(S[name + "_std"], t + 1)
                V.reciprocal(rstd[:, k:k + 1], std[:, k:k + 1]).then_inc(S[name + "_rstd"], 1)
                dve.wait_ge(S[name + "_rstd"], t + 1)
                V.tensor_scalar(dst, x, mv[:, k, 0:1], rstd[:, k:k + 1], ALU.subtract, ALU.mult).then_inc(S[done], 1)

            def front_1(t):
                dve.wait_ge(S["h_taken"], t + 1)
                norm_stats(0, h_cur[:], "ln1", t)

            def front_2(t):
                normalise(0, hn[:], h_cur[:], "ln1", "hn", t)

            def front_3(t):
                dve.wait_ge(S["attn_ps"], t + 1)
                V.tensor_tensor(y[:], small[:, 1, :], hn[:], ALU.add).then_inc(S["y"], 1)
                dve.wait_ge(S["y"], t + 1)
                norm_stats(1, y[:], "ln2", t)

            def front_4(t):
                normalise(1, yn[:], y[:], "ln2", "y_norm", t)

            def front_5(t):
                dve.wait_ge(S["h2"], t + 1)
                norm_stats(2, h2[:], "ln3", t)

            def front_6(t):
                normalise(2, hn2[:], h2[:], "ln3", "hn2", t)

            def front_7(t):
                dve.wait_ge(S["norms_copied"], t + 1)
                V.tensor_scalar(floor_n[:], var_n[:, 0:NH], TINY, TINY * EPS, ALU.mult, ALU.add).then_inc(S["norm_a"], 1)
                dve.wait_ge(S["norm_a"], t + 1)
                V.tensor_tensor(norm2[:], var_n[:, NH:NH + LISTS].rearrange("p (h l) -> p h l", l=2),
                                floor_n[:].rearrange("p (h o) -> p h o", o=1).broadcast_to([P, NH, 2]),
                                ALU.max).then_inc(S["norm_b"], 1)

            def front_8(t):
                dve.wait_ge(S["norm_std"], t + 1)
                reuse(dve, S["handed"], 3 * t)
                V.reciprocal(normr[:], normv[:]).then_inc(S["norm_r"], 1)

            def lists_1(t):
                dve.wait_ge(S["scores_sb"], t + 1)
                reuse(dve, S["sorted_s"], t)
                stand_alone(dve)
                for n in range(LISTS):
                    V.max(top[:, n, 0:8], scores[:, n, :]).then_inc(S["top_a"], 1)

            def lists_2(t):
                reuse(dve, S["idx_f"], t)
                dve.wait_ge(S["top_a"], LISTS * t + LISTS)
                stand_alone(dve)
                for n in range(LISTS):
                    V.max_index(idx[:, n, 0:8], top[:, n, 0:8], scores[:, n, :]).then_inc(S["idx_a"], 1)

            def lists_3(t):
                for n in range(LISTS):
                    V.match_replace(rest[:, n, :], top[:, n, 0:8], scores[:, n, :], LOW).then_inc(S["rest_a"], 1)

            def lists_4(t):
                dve.wait_ge(S["rest_a"], LISTS * t + LISTS)
                stand_alone(dve)
                for n in range(LISTS):
                    V.max(top[:, n, 8:16], rest[:, n, :]).then_inc(S["top_b"], 1)

            def lists_5(t):
                dve.wait_ge(S["top_b"], LISTS * t + LISTS)
                stand_alone(dve)
                for n in range(LISTS):
                    V.max_index(idx[:, n, 8:16], top[:, n, 8:16], rest[:, n, :]).then_inc(S["idx_b"], 1)

            def choose(t):
                dve.wait_ge(S["cells_a"], len(CELLS) * (t + 1))
                stand_alone(dve)
                for h in range(NH):
                    V.max(ctop[:, h, 0:8], cell[:, 0, h, :]).then_inc(S["fin_a"], 1)
                dve.wait_ge(S["fin_a"], NH * t + NH)
                stand_alone(dve)
                for h in range(NH):
                    V.match_replace(crest[:, h, :], ctop[:, h, 0:8], cell[:, 0, h, :], LOW).then_inc(S["fin_rest"], 1)
                dve.wait_ge(S["fin_rest"], NH * t + NH)
                stand_alone(dve)
                for h in range(NH):
                    V.max(ctop[:, h, 8:16], crest[:, h, :]).then_inc(S["fin_b"], 1)
                dve.wait_ge(S["fin_b"], NH * t + NH)
                stand_alone(dve)
                for h in range(NH):
                    V.match_replace(clast[:, h, :], ctop[:, h, 8:16], crest[:, h, :], LOW).then_inc(S["fin_last"], 1)
                dve.wait_ge(S["fin_last"], NH * t + NH)
                reuse(dve, S["masked"], t)
                V.tensor_scalar(sel[:], clast[:], 0.5 * LOW, None, ALU.is_lt).then_inc(S["sel"], 1)

            def weigh(t):
                dve.wait_ge(S["kept"], len(KEPT) * (t + 1))
                V.tensor_reduce(zs[:], slot[:, 1], AX_X, ALU.add).then_inc(S["zsum"], 1)
                bins = slot[:, 0].rearrange("p h s -> p (h s)")
                V.tensor_scalar(hi0[:], bins, 1.0 / LO, 0.5 / LO - 0.5, ALU.mult, ALU.add).then_inc(S["hi_a"], 1)
                dve.wait_ge(S["zsum"], t + 1)
                V.reciprocal(zr[:], zs[:]).then_inc(S["zrec"], 1)
                dve.wait_ge(S["hi_a"], t + 1)
                reuse(dve, S["ktB_ps"], t)
                V.tensor_scalar(parts[:, SPLIT, :], hi0[:], MAGIC, -MAGIC, ALU.add, ALU.add).then_inc(S["hi_f"], 1)
                dve.wait_ge(S["hi_f"], t + 1)
                V.scalar_tensor_tensor(parts[:, SPLIT + 1, :], parts[:, SPLIT, :], -float(LO), bins,
                                       ALU.mult, ALU.add).then_inc(S["lo_f"], 1)

            def one_hots(t):
                dve.wait_ge(S["ktB"], t + 1)
                reuse(dve, S["hist_ps"], 2 * t)
                hi = kt[:, SPLIT].rearrange("p c t -> p (c t)")
                lo = kt[:, SPLIT + 1].rearrange("p c t -> p (c t)")
                for i in range(HI):
                    last = V.tensor_scalar(ohhi[:, i, :], hi, float(i), None, ALU.is_equal)
                last.then_inc(S["oh_hi"], 1)
                for i in range(LO):
                    last = V.tensor_scalar(ohlo[:, :, i, :], lo.rearrange("p (g q) -> p g q", q=GRP), float(i), None, ALU.is_equal)
                last.then_inc(S["oh_lo"], 1)
                dve.wait_ge(S["oh_hi"], t + 1)
                dve.wait_ge(S["ktA"], t + 1)
                for s in range(SPLIT):
                    last = V.tensor_tensor(wh[:, s], kt[:, s:s + 1].rearrange("p s c t -> p s (c t)")
                                           .broadcast_to([P, HI, 2 * P]), ohhi[:], ALU.mult)
                last.then_inc(S["wh"], 1)

            def finish(t):
                dve.wait_ge(S["out_ps"], t + 1)
                dve.wait_ge(S["h_out_stored"], 16 * BPT * t)
                V.tensor_tensor(out_sb[:], fifth[:, 0:D], h2b[:], ALU.add).then_inc(S["out_sb"], 1)

            def step(i):
                n = i + 1
                front_1(n)
                lists_1(i)
                front_2(n)
                lists_2(i)
                lists_3(i)
                front_3(n)
                lists_4(i)
                front_4(n)
                lists_5(i)
                front_5(n)
                front_6(n)
                choose(i)
                front_7(n)
                weigh(i)
                one_hots(i)
                finish(i)
                front_8(n)

            front_1(0)
            front_2(0)
            front_3(0)
            front_4(0)
            front_5(0)
            front_6(0)
            front_7(0)
            front_8(0)
            step(0)
            with dve.Fori(1, TILES - 1) as i:
                step(i)
            n = TILES - 1
            lists_1(n)
            lists_2(n)
            lists_3(n)
            lists_4(n)
            lists_5(n)
            choose(n)
            weigh(n)
            one_hots(n)
            finish(n)

        @block.gpsimd
        def _(pool):
            G = nc.gpsimd
            G.memset(ones[:], 1.0).then_inc(S["setup_pool"], 1)
            G.memset(eps[:], EPS).then_inc(S["setup_pool"], 1)
            G.memset(kbd[:], 0.0).then_inc(S["setup_pool"], 1)
            G.memset(gated[:], 0.0).then_inc(S["setup_pool"], 1)
            pool.wait_ge(S["weights"], 16 * len(WLOADS))

            def take(t, loaded):
                pool.wait_ge(S["h_loaded"], loaded)
                reuse(pool, S["h2"], t)
                stand_alone(pool)
                G.tensor_copy(h_cur[:], h_in[:]).then_inc(S["h_taken"], 1)

            def hand_over(t):
                pool.wait_ge(S["expert_act"], t + 1)
                pool.wait_ge(S["norm_r"], t + 1)
                reuse(pool, S["out_sb"], t)
                stand_alone(pool)
                G.tensor_copy(h2b[:], h2[:]).then_inc(S["handed"], 1)
                G.tensor_tensor(eactb[:].rearrange("p i (g q) -> p (i g) q", q=GRP), eact[:].rearrange("p i (g q) -> p (i g) q", q=GRP),
                                qmask[:].rearrange("p (o q) -> p o q", o=1).broadcast_to([P, HI * NGRP, GRP]), ALU.mult).then_inc(S["handed"], 1)
                G.tensor_copy(normb[:], normr[:]).then_inc(S["handed"], 1)

            def front(t):
                pool.wait_ge(S["qk_exp"], t + 1)
                pool.wait_ge(S["qk_pos"], t + 1)
                G.tensor_tensor(qk[:].rearrange("p c i -> p (c i)"), ex[:], pos[:], ALU.add).then_inc(S["qk"], 1)
                pool.wait_ge(S["at_copied"], t + 1)
                G.tensor_tensor(atm[:], at[:], mask[:].rearrange("p (o i) -> p o i", o=1).broadcast_to([P, NH, P]),
                                ALU.mult).then_inc(S["at_masked"], 1)

            def front_end(t):
                pool.wait_ge(S["y_norm"], t + 1)
                G.tensor_tensor(yg[:], yn[:], gam[:], ALU.mult).then_inc(S["y_gamma"], 1)
                pool.wait_ge(S["y_gamma"], t + 1)
                G.tensor_tensor(yb[:], yg[:], bet[:], ALU.add).then_inc(S["y_beta"], 1)
                pool.wait_ge(S["y_beta"], t + 1)
                G.tensor_tensor(h2[:], yb[:], h_cur[:], ALU.add).then_inc(S["h2"], 1)

            def cells(k, src, op, sem, t):
                for a, rows, cols, first in CELLS:
                    kinds = src.shape[1]
                    lhs = src[:, :, 0, a:a + rows].rearrange("p k (a o) -> p k a o", o=1).broadcast_to([P, kinds, rows, cols])
                    rhs = src[:, :, 1, 0:cols].rearrange("p k (o b) -> p k o b", o=1).broadcast_to([P, kinds, rows, cols])
                    dst = cell[:].rearrange("p k h n -> p (k h) n")[:, k * NH:k * NH + kinds, first:first + rows * cols]
                    G.tensor_tensor(dst.rearrange("p k (a b) -> p k a b", a=rows), lhs, rhs, op).then_inc(sem, 1)

            def back(t):
                pool.wait_ge(S["top_b"], LISTS * t + LISTS)
                pool.wait_ge(S["handed"], 3 * t + 3)
                G.tensor_tensor(sv[:, 0], top[:], normb[:].rearrange("p (l o) -> p l o", o=1)
                                .broadcast_to([P, LISTS, TOPK]), ALU.mult).then_inc(S["sorted_s"], 1)
                pool.wait_ge(S["sorted_s"], t + 1)
                G.tensor_tensor(sh[:], sv[:, 0], sv[:, 0, :, 0:1].broadcast_to([P, LISTS, TOPK]),
                                ALU.subtract).then_inc(S["shifted"], 1)
                pool.wait_ge(S["idx_f"], t + 1)
                cells(0, sv[:].rearrange("p k (h l) n -> p (k h) l n", l=2), ALU.add, S["cells_a"], t)
                pool.wait_ge(S["exps"], t + 1)
                cells(2, es[:].rearrange("p (h l) n -> p h l n", l=2), ALU.mult, S["cells_w"], t)
                pool.wait_ge(S["cells_w"], len(CELLS) * (t + 1))
                pool.wait_ge(S["cells_a"], len(CELLS) * (t + 1))
                pool.wait_ge(S["sel"], t + 1)
                reuse(pool, S["kept"], len(KEPT) * t)
                G.tensor_tensor(chosen[:].rearrange("p (k h) n -> p k (h n)", k=2),
                                cell[:, 1:3].rearrange("p k h n -> p k (h n)"),
                                sel[:].rearrange("p h n -> p (h n)").rearrange("p (o n) -> p o n", o=1)
                                .broadcast_to([P, 2, NH * NCELL]), ALU.mult).then_inc(S["masked"], 1)
                pool.wait_ge(S["masked"], t + 1)
                for src, step, count, dst in FOLDS:
                    frm = chosen[:, :, src:src + step * (count - 1) + 1:step]
                    to = chosen[:, :, dst:dst - count:-1]
                    G.tensor_tensor(to, to, frm, ALU.add).then_inc(S["folded"], 1)
                pool.wait_ge(S["zrec"], t + 1)
                G.tensor_tensor(wn[:].rearrange("p (h s) -> p h s", h=NH), slot[:, 1],
                                zr[:].rearrange("p (h o) -> p h o", o=1).broadcast_to([P, NH, NSLOT]),
                                ALU.mult).then_inc(S["wnorm"], 1)
                pool.wait_ge(S["w1"], t + 1)
                G.tensor_tensor(r1[:], wn[:], parts[:, 0, :], ALU.subtract).then_inc(S["r1"], 1)
                pool.wait_ge(S["w2"], t + 1)
                G.tensor_tensor(parts[:, 2, :], r1[:], parts[:, 1, :], ALU.subtract).then_inc(S["w3"], 1)
                pool.wait_ge(S["hist_sb"], 4 * t + 4)
                hsf = hs[:].rearrange("p s i t -> p s (i t)")
                G.tensor_tensor(gs[:, 0], hsf[:, 0], hsf[:, 1], ALU.add).then_inc(S["g_a"], 1)
                pool.wait_ge(S["g_a"], t + 1)
                G.tensor_tensor(gs[:, 1], gs[:, 0], hsf[:, 2], ALU.add).then_inc(S["g_sum"], 1)
                pool.wait_ge(S["g_sum"], t + 1)
                G.tensor_tensor(gated[:].rearrange("p i t -> p (i t)"), gs[:, 1], eactb[:].rearrange("p i t -> p (i t)"),
                                ALU.mult).then_inc(S["gated"], 1)

            def step(i):
                take(i + 1, loads(i + 1))
                front(i + 1)
                hand_over(i)
                front_end(i + 1)
                back(i)

            take(0, loads(0))
            front(0)
            front_end(0)
            step(0)
            with pool.Fori(1, TILES - 1) as i:
                step(i)
            hand_over(TILES - 1)
            back(TILES - 1)


def loads(t):
    return 16 * BPT * (t + 1)


_OUTS = [((STEPS, NPOS, D), 'float32')]


def kernel(**inputs):
    import numpy as _np
    import concourse.bacc as _bacc
    from concourse import mybir as _mybir
    from concourse.bass_utils import run_bass_kernel_spmd as _run

    f = {k: _np.asarray(v) for k, v in inputs.items()}
    f32 = _np.float32
    two = _np.arange(P) // DH
    quad = _np.arange(P) // 32
    t_blk, t_step = _np.arange(P) // STEPS, _np.arange(P) % STEPS
    same = (two[:, None] == two[None, :]).astype(f32)
    ind8 = _np.zeros((P, CH, NH), f32)
    for c in range(CH):
        ind8[_np.arange(P), c, 2 * c + two] = 1.0 / DH
    x = f['x'].reshape(STEPS, 3, 4, 16, 4, 16).transpose(1, 3, 5, 2, 4, 0).reshape(KCH, P, TOK_TILES * P)
    arrays = {
        'xT': x.transpose(1, 0, 2),
        'txt': f['txt'],
        'identity': _np.eye(P, dtype=f32),
        'causal': ((t_blk[:, None] == t_blk[None, :]) & (t_step[:, None] <= t_step[None, :])).astype(f32),
        'centre': _np.eye(P, dtype=f32) - same / DH,
        'ind8': ind8,
        'ind4': (quad[:, None] == _np.arange(4)[None, :]).astype(f32),
        'headmask': _np.kron(_np.eye(NH, dtype=f32), _np.ones((1, DH), f32)),
        'tok_wT': f['L0_tok_w'].reshape(D, KCH, P).transpose(2, 1, 0),
        'tok_b': f['L0_tok_b'].reshape(1, D),
        'wqkT': _np.concatenate([f['L0_attn_Wq'], f['L0_attn_Wkv'][:NH * DH]], 0).T,
        'wvT': f['L0_attn_Wkv'][NH * DH:].T,
        'woT': f['L0_attn_Wo'].reshape(D, CH, P).transpose(2, 1, 0),
        'gamma': f['L0_attn_ln_gamma'].reshape(1, D),
        'beta': f['L0_attn_ln_beta'].reshape(1, D),
        'ffn_wq': f['L0_ffn_Wq'].reshape(CH, P, D).transpose(1, 0, 2),
        'ffn_bq': f['L0_ffn_bq'].reshape(CH, P).T,
        'ln_g': _np.concatenate([f['L0_ffn_ln_g']] * 2).reshape(1, P),
        'ln_b': _np.concatenate([f['L0_ffn_ln_b']] * NH).reshape(1, NH * DH),
        'keys': _np.stack([_np.stack([f['L0_ffn_keys0'], f['L0_ffn_keys1']], 1)] * 2, 1),
        'downT': _np.repeat(f['L0_ffn_expert_down'][:HI * LO].T.reshape(D, HI, LO), GRP, 2),
        'up': _np.repeat(f['L0_ffn_expert_up'][:HI * LO].reshape(HI, LO, D).transpose(1, 0, 2), GRP, 0),
        'groupmask': (_np.arange(P)[:, None] % GRP == _np.arange(GRP)[None, :]).astype(f32),
    }
    nc = _bacc.Bacc("TRN2", target_bir_lowering=False, num_devices=1)
    feeds, args = {}, []
    for name, a in arrays.items():
        a = _np.ascontiguousarray(a)
        feeds[f"in_{name}_dram"] = a
        args.append(nc.dram_tensor(f"in_{name}_dram", a.shape, _mybir.dt.from_np(a.dtype), kind="ExternalInput").ap())
    for i, (shape, dtype) in enumerate(_OUTS):
        dt = _mybir.dt.from_np(_np.dtype(dtype))
        args.append(nc.dram_tensor(f"out_{i}_dram", shape, dt, kind="ExternalOutput").ap())
    build(nc, *args)
    r = _run(nc, [feeds], core_ids=[0])
    return r.results[0]["out_0_dram"]
```
